# Optimizing a Trainium2 kernel written in Bass

```python
import numpy as np
import jax
import jax.numpy as jnp

def _softmax(x, axis=-1):
    return jax.nn.softmax(x, axis=axis)

def _gelu(x):
    return jax.nn.gelu(x, approximate=True)

def _silu(x):
    return jax.nn.silu(x)

def _sigmoid(x):
    return jax.nn.sigmoid(x)

def _layernorm(x, axis=-1, eps=1e-05):
    m = jnp.mean(x, axis=axis, keepdims=True)
    v = jnp.var(x, axis=axis, keepdims=True)
    return (x - m) / jnp.sqrt(v + eps)

def _scatter_add(tgt, idx, src, axis=0):
    return tgt.at[idx].add(src)

def _segment_sum(src, seg, n):
    return jax.ops.segment_sum(src, seg, n)
kernel_name = 'mk_dlrm_tower_d1_rec_r8_7f0ed8'

def setup_inputs(seed: int=0):
    np.random.seed(seed)
    _w = jnp.asarray

    def _rec_inputs():
        import jax
        import jax.numpy as jnp
        _tk = jax.random.key(seed)
        ids = jnp.stack([jax.random.randint(jax.random.fold_in(_tk, 200 + f), (512,), 0, v, jnp.int32) for f, v in enumerate([1000, 1250, 12500, 125000, 1250, 1000, 1250, 1000, 1250, 12500, 1250, 1250, 1250, 1000, 12500, 1000, 12500, 1250, 12500, 1000, 1000, 1000, 1000, 12500, 1250, 1250])], axis=1)
        tbl_0 = 0.05 * jax.random.normal(jax.random.fold_in(_tk, 500 + 0), (1000, 128), jnp.float32)
        tbl_1 = 0.05 * jax.random.normal(jax.random.fold_in(_tk, 500 + 1), (1250, 128), jnp.float32)
        tbl_2 = 0.05 * jax.random.normal(jax.random.fold_in(_tk, 500 + 2), (12500, 128), jnp.float32)
        tbl_3 = 0.05 * jax.random.normal(jax.random.fold_in(_tk, 500 + 3), (125000, 128), jnp.float32)
        tbl_4 = 0.05 * jax.random.normal(jax.random.fold_in(_tk, 500 + 4), (1250, 128), jnp.float32)
        tbl_5 = 0.05 * jax.random.normal(jax.random.fold_in(_tk, 500 + 5), (1000, 128), jnp.float32)
        tbl_6 = 0.05 * jax.random.normal(jax.random.fold_in(_tk, 500 + 6), (1250, 128), jnp.float32)
        tbl_7 = 0.05 * jax.random.normal(jax.random.fold_in(_tk, 500 + 7), (1000, 128), jnp.float32)
        tbl_8 = 0.05 * jax.random.normal(jax.random.fold_in(_tk, 500 + 8), (1250, 128), jnp.float32)
        tbl_9 = 0.05 * jax.random.normal(jax.random.fold_in(_tk, 500 + 9), (12500, 128), jnp.float32)
        tbl_10 = 0.05 * jax.random.normal(jax.random.fold_in(_tk, 500 + 10), (1250, 128), jnp.float32)
        tbl_11 = 0.05 * jax.random.normal(jax.random.fold_in(_tk, 500 + 11), (1250, 128), jnp.float32)
        tbl_12 = 0.05 * jax.random.normal(jax.random.fold_in(_tk, 500 + 12), (1250, 128), jnp.float32)
        tbl_13 = 0.05 * jax.random.normal(jax.random.fold_in(_tk, 500 + 13), (1000, 128), jnp.float32)
        tbl_14 = 0.05 * jax.random.normal(jax.random.fold_in(_tk, 500 + 14), (12500, 128), jnp.float32)
        tbl_15 = 0.05 * jax.random.normal(jax.random.fold_in(_tk, 500 + 15), (1000, 128), jnp.float32)
        tbl_16 = 0.05 * jax.random.normal(jax.random.fold_in(_tk, 500 + 16), (12500, 128), jnp.float32)
        tbl_17 = 0.05 * jax.random.normal(jax.random.fold_in(_tk, 500 + 17), (1250, 128), jnp.float32)
        tbl_18 = 0.05 * jax.random.normal(jax.random.fold_in(_tk, 500 + 18), (12500, 128), jnp.float32)
        tbl_19 = 0.05 * jax.random.normal(jax.random.fold_in(_tk, 500 + 19), (1000, 128), jnp.float32)
        tbl_20 = 0.05 * jax.random.normal(jax.random.fold_in(_tk, 500 + 20), (1000, 128), jnp.float32)
        tbl_21 = 0.05 * jax.random.normal(jax.random.fold_in(_tk, 500 + 21), (1000, 128), jnp.float32)
        tbl_22 = 0.05 * jax.random.normal(jax.random.fold_in(_tk, 500 + 22), (1000, 128), jnp.float32)
        tbl_23 = 0.05 * jax.random.normal(jax.random.fold_in(_tk, 500 + 23), (12500, 128), jnp.float32)
        tbl_24 = 0.05 * jax.random.normal(jax.random.fold_in(_tk, 500 + 24), (1250, 128), jnp.float32)
        tbl_25 = 0.05 * jax.random.normal(jax.random.fold_in(_tk, 500 + 25), (1250, 128), jnp.float32)
        _rk = jax.random.fold_in(_tk, 7)
        r_bottom_output = -0.000520686 + 1.00062 * jax.random.normal(jax.random.fold_in(_rk, 101), (512, 128), jnp.float32)
        W_top1 = 0.0456912 * jax.random.normal(jax.random.fold_in(_tk, 801), (479, 512), jnp.float32)
        W_top2 = 0.0441942 * jax.random.normal(jax.random.fold_in(_tk, 802), (512, 256), jnp.float32)
        W_top3 = 0.0625 * jax.random.normal(jax.random.fold_in(_tk, 803), (256, 1), jnp.float32)
        b_top1 = jnp.zeros((512,), jnp.float32)
        b_top2 = jnp.zeros((256,), jnp.float32)
        return (r_bottom_output, ids, tbl_0, tbl_1, tbl_2, tbl_3, tbl_4, tbl_5, tbl_6, tbl_7, tbl_8, tbl_9, tbl_10, tbl_11, tbl_12, tbl_13, tbl_14, tbl_15, tbl_16, tbl_17, tbl_18, tbl_19, tbl_20, tbl_21, tbl_22, tbl_23, tbl_24, tbl_25, W_top1, b_top1, W_top2, b_top2, W_top3)
    r_bottom_output, ids, tbl_0, tbl_1, tbl_2, tbl_3, tbl_4, tbl_5, tbl_6, tbl_7, tbl_8, tbl_9, tbl_10, tbl_11, tbl_12, tbl_13, tbl_14, tbl_15, tbl_16, tbl_17, tbl_18, tbl_19, tbl_20, tbl_21, tbl_22, tbl_23, tbl_24, tbl_25, W_top1, b_top1, W_top2, b_top2, W_top3 = _rec_inputs()

    def _L0_rec_setup():
        import jax, jax.numpy as jnp
        import numpy as np
        NUM_FEATURES = 27
        _TRIU_I, _TRIU_J = np.triu_indices(NUM_FEATURES, k=1)
        key = jax.random.key(seed)
        k1, k2 = jax.random.split(key)
        bottom_output = jax.random.normal(k1, (2048, 128), dtype=jnp.float32)
        embeddings = jax.random.normal(k2, (2048, 26, 128), dtype=jnp.float32)
        return {'bottom_output': bottom_output, 'embeddings': embeddings}
    _L0_rec_all = _L0_rec_setup()
    _L0_rec_in = {k: v for k, v in _L0_rec_all.items() if k in ()}
    del _L0_rec_all
    return {'r_bottom_output': r_bottom_output, 'ids': ids, 'tbl_0': tbl_0, 'tbl_1': tbl_1, 'tbl_2': tbl_2, 'tbl_3': tbl_3, 'tbl_4': tbl_4, 'tbl_5': tbl_5, 'tbl_6': tbl_6, 'tbl_7': tbl_7, 'tbl_8': tbl_8, 'tbl_9': tbl_9, 'tbl_10': tbl_10, 'tbl_11': tbl_11, 'tbl_12': tbl_12, 'tbl_13': tbl_13, 'tbl_14': tbl_14, 'tbl_15': tbl_15, 'tbl_16': tbl_16, 'tbl_17': tbl_17, 'tbl_18': tbl_18, 'tbl_19': tbl_19, 'tbl_20': tbl_20, 'tbl_21': tbl_21, 'tbl_22': tbl_22, 'tbl_23': tbl_23, 'tbl_24': tbl_24, 'tbl_25': tbl_25, 'W_top1': W_top1, 'b_top1': b_top1, 'W_top2': W_top2, 'b_top2': b_top2, 'W_top3': W_top3}

def reference(r_bottom_output, ids, tbl_0, tbl_1, tbl_2, tbl_3, tbl_4, tbl_5, tbl_6, tbl_7, tbl_8, tbl_9, tbl_10, tbl_11, tbl_12, tbl_13, tbl_14, tbl_15, tbl_16, tbl_17, tbl_18, tbl_19, tbl_20, tbl_21, tbl_22, tbl_23, tbl_24, tbl_25, W_top1, b_top1, W_top2, b_top2, W_top3):
    import jax
    import jax.numpy as jnp

    def _L0_rec_ref(bottom_output, embeddings):
        import jax, jax.numpy as jnp
        import numpy as np
        NUM_FEATURES = 27
        _TRIU_I, _TRIU_J = np.triu_indices(NUM_FEATURES, k=1)
        all_emb = jnp.concatenate([bottom_output[:, None, :], embeddings], axis=1)
        gram = jnp.einsum('bfd,bgd->bfg', all_emb, all_emb)
        return gram[:, _TRIU_I, _TRIU_J]
    e = jnp.stack([tbl_0[ids[:, 0]], tbl_1[ids[:, 1]], tbl_2[ids[:, 2]], tbl_3[ids[:, 3]], tbl_4[ids[:, 4]], tbl_5[ids[:, 5]], tbl_6[ids[:, 6]], tbl_7[ids[:, 7]], tbl_8[ids[:, 8]], tbl_9[ids[:, 9]], tbl_10[ids[:, 10]], tbl_11[ids[:, 11]], tbl_12[ids[:, 12]], tbl_13[ids[:, 13]], tbl_14[ids[:, 14]], tbl_15[ids[:, 15]], tbl_16[ids[:, 16]], tbl_17[ids[:, 17]], tbl_18[ids[:, 18]], tbl_19[ids[:, 19]], tbl_20[ids[:, 20]], tbl_21[ids[:, 21]], tbl_22[ids[:, 22]], tbl_23[ids[:, 23]], tbl_24[ids[:, 24]], tbl_25[ids[:, 25]]], axis=1)
    z = _L0_rec_ref(r_bottom_output, e)
    z = z.reshape(z.shape[0], -1)
    h = jnp.concatenate([z, r_bottom_output], axis=1)
    h = jnp.maximum(h @ W_top1 + b_top1, 0.0)
    h = jnp.maximum(h @ W_top2 + b_top2, 0.0)
    y = h @ W_top3
    return y

_drawn_inputs = setup_inputs


def setup_inputs(seed=0):
    import zlib

    import numpy as np

    out = dict(_drawn_inputs(seed))
    spreads = {'b_top1': (0.0, 0.1), 'b_top2': (0.0, 0.1)}
    factors = {}
    for name, (base, spread) in spreads.items():
        noise = np.random.default_rng([zlib.crc32(name.encode()), seed]).standard_normal(out[name].shape)
        drawn = base * np.exp(spread * noise) if base else spread * noise
        out[name] = jnp.asarray(drawn.astype(out[name].dtype))
    for name, factor in factors.items():
        out[name] = (out[name] * factor).astype(out[name].dtype)
    return out
```

```python
import concourse.bass as bass
from concourse import mybir
from contextlib import ExitStack


def dlrm_tower_kernel(nc, r_dram, ids_dram, tables, w1_pairs_dram, w1_bottom_dram, b1_dram, w2_dram, b2_dram,
                      w3_dram, y_dram):
    fp32, i32 = mybir.dt.float32, mybir.dt.int32
    ALU = mybir.AluOpType
    ACT = mybir.ActivationFunctionType

    BATCH, NTAB = ids_dram.shape
    D = r_dram.shape[1]
    NF = NTAB + 1
    FP = 32
    TB = 128
    TILES = BATCH // TB
    SG = TB // FP
    NQ = TB // SG
    HALF = NF // 2
    KC = HALF + 1
    CH = 3
    KR = KC * NF // CH
    H1 = w1_bottom_dram.shape[1]
    H2 = w2_dram.shape[1]
    O1, O2 = H1 // 128, H2 // 128
    GRP = 4
    GROUPS = [list(range(a, min(a + GRP, NF))) for a in range(0, NF, GRP)]
    NG = len(GROUPS)
    UQ = 8
    UNITS = NQ // UQ
    BANK = 512

    ctx = ExitStack()
    with ctx:
        def sb(name, shape, dt=fp32):
            return ctx.enter_context(nc.sbuf_tensor(name, shape, dt))

        def sem(name):
            return ctx.enter_context(nc.semaphore(name))

        ids_all = sb("ids_all", [TB, TILES, NTAB], i32)
        raw = sb("raw", [TB, NF, D])
        feat_t = sb("feat_t", [D, NQ, SG, FP])
        gram = sb("gram", [128, NQ, KC])
        pairs = sb("pairs", [TB, KC * FP])
        pairs_packed = sb("pairs_packed", [TB, KC * NF])
        pairs_t = sb("pairs_t", [KR, CH, TB])
        w1_pairs = sb("w1_pairs", [KR, CH, H1])
        w1_bottom = sb("w1_bottom", [D, H1])
        w2 = sb("w2", [128, O1, H2])
        w3 = sb("w3", [128, O2])
        b1 = sb("b1", [128, O1])
        b2 = sb("b2", [128, O2])
        h1 = sb("h1", [128, O1, TB])
        h2 = sb("h2", [128, O2, TB])
        y_row = sb("y_row", [1, BATCH])
        ident = sb("ident", [128, 128])
        second = sb("second", [128, UQ, HALF], i32)
        act_warm = sb("act_warm", [128, 1])

        turn = [ctx.enter_context(nc.psum_tensor(f"turn{i}", [128, BANK], fp32)) for i in range(2)]
        dots = [ctx.enter_context(nc.psum_tensor(f"dots{i}", [128, UQ, 128], fp32)) for i in range(2)]
        acc1 = [ctx.enter_context(nc.psum_tensor(f"acc1_{i}", [128, BANK], fp32)) for i in range(2)]

        ids_in = sem("ids_in")
        bottom_in = sem("bottom_in")
        group_in = [sem(f"group_in{g}") for g in range(NG)]
        tower_in = sem("tower_in")
        ones_set = sem("ones_set")
        ident_ready = sem("ident_ready")
        mask_quadrant = sem("mask_quadrant")
        mask_ready = sem("mask_ready")
        transposed = sem("transposed")
        feat_dve = sem("feat_dve")
        feat_act = sem("feat_act")
        unit_done = sem("unit_done")
        first_copied = sem("first_copied")
        folded = sem("folded")
        pairs_ready = sem("pairs_ready")
        pairs_packed_ready = sem("pairs_packed_ready")
        pairs_turned = sem("pairs_turned")
        pairs_t_ready = sem("pairs_t_ready")
        acc1_done = sem("acc1_done")
        h1_act = sem("h1_act")
        h1_dve = sem("h1_dve")
        acc2_done = sem("acc2_done")
        h2_ready = sem("h2_ready")
        y_done = sem("y_done")
        y_ready = sem("y_ready")
        y_out = sem("y_out")

        EVEN = (NG + 1) // 2
        ODD = NG // 2

        block = ctx.enter_context(nc.Block())

        @block.sync
        def _(sp):
            sp.dma_start(ids_all[:], ids_dram.rearrange("(t p) f -> p t f", p=TB)).then_inc(ids_in, 16)
            sp.dma_start(raw[:, 0, :], r_dram[0:TB, :]).then_inc(bottom_in, 16)
            sp.dma_start(w1_pairs[:], w1_pairs_dram.rearrange("(c k) n -> k c n", c=CH)).then_inc(tower_in, 16)
            sp.dma_start(w1_bottom[:], w1_bottom_dram).then_inc(tower_in, 16)
            sp.dma_start(w2[:], w2_dram.rearrange("(c p) n -> p c n", p=128)).then_inc(tower_in, 16)
            with nc.allow_non_contiguous_dma(reason="one column of a few hundred values, once"):
                sp.dma_start(w3[:], w3_dram.rearrange("(c p) one -> p (c one)", p=128)).then_inc(tower_in, 16)
                sp.dma_start(b1[:], b1_dram.rearrange("(c p) -> p c", p=128)).then_inc(tower_in, 16)
                sp.dma_start(b2[:], b2_dram.rearrange("(c p) -> p c", p=128)).then_inc(tower_in, 16)
            for t in range(1, TILES):
                sp.wait_ge(transposed, t * NG - NG + 1)
                sp.dma_start(raw[:, 0, :], r_dram[t * TB:(t + 1) * TB, :]).then_inc(bottom_in, 16)
            sp.wait_ge(y_ready, TILES)
            sp.dma_start(y_dram, y_row[:]).then_inc(y_out, 16)
            sp.wait_ge(y_out, 16)

        @block.gpsimd
        def _(pool):
            nc.gpsimd.memset(ident[:], 1.0)
            nc.gpsimd.memset(second[0:FP], 1).then_inc(ones_set, 1)
            pool.wait_ge(ones_set, 1)
            nc.gpsimd.affine_select(out=ident[:], in_=ident[:], compare_op=ALU.is_equal, fill=0.0, base=0,
                                    pattern=[[-1, 128]], channel_multiplier=1).then_inc(ident_ready, 1)
            nc.gpsimd.affine_select(out=second[0:FP], in_=second[0:FP], compare_op=ALU.is_gt, fill=0.0, base=0,
                                    pattern=[[0, UQ], [-1, HALF]], channel_multiplier=1).then_inc(ones_set, 1)
            pool.wait_ge(ones_set, 2)
            nc.gpsimd.affine_select(out=second[0:FP], in_=second[0:FP], compare_op=ALU.is_ge, fill=0.0, base=HALF,
                                    pattern=[[0, UQ], [1, HALF]], channel_multiplier=-1).then_inc(mask_quadrant, 1)

            pool.wait_ge(ids_in, 16)
            for t in range(TILES):
                for g, fs in enumerate(GROUPS):
                    if t > 0:
                        pool.wait_ge(transposed, (t - 1) * NG + g + 1)
                    for f in fs:
                        if f > 0:
                            nc.gpsimd.indirect_dma_start(
                                out=raw[:, f, :], out_offset=None, in_=tables[f - 1],
                                in_offset=bass.IndirectOffsetOnAxis(ap=ids_all[:, t, f - 1:f], axis=0),
                            ).then_inc(group_in[g], 16)

        def feature_dst(g):
            fs = GROUPS[g]
            return feat_t[:, :, :, fs[0]:fs[-1] + 1].rearrange("d q s f -> d f s q")

        def feature_src(g):
            return turn[g % 2][:, 0:len(GROUPS[g]) * TB].rearrange("d (f s q) -> d f s q", s=SG, q=NQ)

        @block.scalar
        def _(act):
            nc.scalar.activation(act_warm[:], nc.const_aps.tensor(0.0, (128, 1)), ACT.Relu).then_inc(feat_act, 1)
            act.wait_ge(tower_in, 6 * 16)
            for t in range(TILES):
                for g in range(1, NG, 2):
                    act.wait_ge(transposed, t * NG + g + 1)
                    nc.scalar.copy(feature_dst(g), feature_src(g)).then_inc(feat_act, 1)
                for u in range(UNITS):
                    act.wait_ge(unit_done, t * UNITS + u + 1)
                    for s in range(SG):
                        own = slice(s * FP, (s + 1) * FP)
                        last = nc.scalar.copy(gram[own, u * UQ:(u + 1) * UQ, :],
                                              dots[u % 2][own, :, s * NF:s * NF + KC])
                    last.then_inc(first_copied, 1)
                act.wait_ge(pairs_ready, t + 1)
                nc.scalar.copy(pairs_packed[:].rearrange("b (k f) -> b k f", f=NF),
                               pairs[:].rearrange("b (k f) -> b k f", f=FP)[:, :, 0:NF]).then_inc(pairs_packed_ready, 1)
                act.wait_ge(pairs_turned, t + 1)
                nc.scalar.copy(pairs_t[:].rearrange("k c b -> k (c b)"),
                               turn[0][0:KR, 0:CH * TB]).then_inc(pairs_t_ready, 1)
                act.wait_ge(acc1_done, t * 2 + 1)
                for o in range(O1 // 2):
                    last = nc.scalar.activation(h1[:, o, :], acc1[0][:, o * TB:(o + 1) * TB], ACT.Relu,
                                                bias=b1[:, o:o + 1])
                last.then_inc(h1_act, 1)
                act.wait_ge(acc2_done, t + 1)
                for o in range(O2):
                    last = nc.scalar.activation(h2[:, o, :], turn[1][:, o * TB:(o + 1) * TB], ACT.Relu,
                                                bias=b2[:, o:o + 1])
                last.then_inc(h2_ready, 1)

        @block.vector
        def _(dve):
            nc.vector.memset(feat_t[:, :, :, NF:FP], 0.0).then_inc(feat_dve, 1)
            dve.wait_ge(mask_quadrant, 1)
            for s in range(1, SG):
                nc.vector.tensor_copy(second[s * FP:(s + 1) * FP], second[0:FP]).then_inc(mask_ready, 1)
            dve.wait_ge(tower_in, 6 * 16)
            for t in range(TILES):
                for g in range(0, NG, 2):
                    dve.wait_ge(transposed, t * NG + g + 1)
                    nc.vector.tensor_copy(feature_dst(g), feature_src(g)).then_inc(feat_dve, 1)
                for u in range(UNITS):
                    dve.wait_ge(first_copied, t * UNITS + u + 1)
                    dve.wait_ge(mask_ready, SG - 1)
                    for s in range(SG):
                        own = slice(s * FP, (s + 1) * FP)
                        last = nc.vector.copy_predicated(gram[own, u * UQ:(u + 1) * UQ, 0:HALF], second[own],
                                                         dots[u % 2][own, :, s * NF + KC:(s + 1) * NF])
                    last.then_inc(folded, 1)
                dve.wait_ge(folded, t * UNITS + UNITS)
                nc.vector.transpose(pairs[:].rearrange("b (k f) -> b k f", f=FP),
                                    gram[:].rearrange("p q k -> p k q")).then_inc(pairs_ready, 1)
                dve.wait_ge(acc1_done, t * 2 + 2)
                for o in range(O1 // 2, O1):
                    at = (o - O1 // 2) * TB
                    last = nc.vector.tensor_scalar(h1[:, o, :], acc1[1][:, at:at + TB], b1[:, o:o + 1], 0.0,
                                                   ALU.add, ALU.max)
                last.then_inc(h1_dve, 1)
                dve.wait_ge(y_done, t + 1)
                nc.vector.tensor_copy(y_row[:, t * TB:(t + 1) * TB], acc1[0][0:1, 0:TB]).then_inc(y_ready, 1)

        @block.tensor
        def _(pe):
            pe.wait_ge(ident_ready, 1)
            for t in range(TILES):
                for g, fs in enumerate(GROUPS):
                    pe.wait_ge(group_in[g], (t + 1) * 16 * (len(fs) - (g == 0)))
                    if g == 0:
                        pe.wait_ge(bottom_in, (t + 1) * 16)
                    if g % 2 == 0:
                        pe.wait_ge(feat_dve, t * EVEN + g // 2 + 1)
                    else:
                        pe.wait_ge(feat_act, t * ODD + g // 2 + 1)
                    for i, f in enumerate(fs):
                        last = nc.tensor.transpose(turn[g % 2][:, i * TB:(i + 1) * TB], raw[:, f, :], ident[:])
                    last.then_inc(transposed, 1)
                pe.wait_ge(feat_dve, t * EVEN + EVEN + 1)
                pe.wait_ge(feat_act, t * ODD + ODD + 1)
                for u in range(UNITS):
                    if u >= 2:
                        pe.wait_ge(folded, t * UNITS + u - 1)
                    for i in range(UQ):
                        q = u * UQ + i
                        last = nc.tensor.matmul(dots[u % 2][:, i, 0:SG * NF],
                                                feat_t[:, q].rearrange("d s f -> d (s f)"),
                                                feat_t[:, q, :, 0:NF], start=True, stop=True)
                    last.then_inc(unit_done, 1)
                pe.wait_ge(pairs_packed_ready, t + 1)
                for c in range(CH):
                    last = nc.tensor.transpose(turn[0][0:KR, c * TB:(c + 1) * TB],
                                               pairs_packed[:, c * KR:(c + 1) * KR], ident[:])
                last.then_inc(pairs_turned, 1)
                bottom_t = feat_t[:, :, :, 0].rearrange("d q s -> d s q")
                pe.wait_ge(tower_in, 6 * 16)
                for o in range(O1):
                    dst = acc1[o // (O1 // 2)][:, (o % (O1 // 2)) * TB:(o % (O1 // 2) + 1) * TB]
                    out_cols = slice(o * 128, (o + 1) * 128)
                    nc.tensor.matmul(dst, w1_bottom[:, out_cols], bottom_t, start=True, stop=False)
                    if o == 0:
                        pe.wait_ge(pairs_t_ready, t + 1)
                    for c in range(CH):
                        last = nc.tensor.matmul(dst, w1_pairs[:, c, out_cols], pairs_t[:, c, :],
                                                start=False, stop=(c == CH - 1))
                    if o % (O1 // 2) == O1 // 2 - 1:
                        last.then_inc(acc1_done, 1)
                pe.wait_ge(h1_act, t + 1)
                pe.wait_ge(h1_dve, t + 1)
                for o in range(O2):
                    for c in range(O1):
                        last = nc.tensor.matmul(turn[1][:, o * TB:(o + 1) * TB], w2[:, c, o * 128:(o + 1) * 128],
                                                h1[:, c, :], start=(c == 0), stop=(c == O1 - 1))
                last.then_inc(acc2_done, 1)
                pe.wait_ge(h2_ready, t + 1)
                for c in range(O2):
                    last = nc.tensor.matmul(acc1[0][0:1, 0:TB], w3[:, c:c + 1], h2[:, c, :],
                                            start=(c == 0), stop=(c == O2 - 1))
                last.then_inc(y_done, 1)


def pair_rows(features):
    half = features // 2
    rows, places = [], []
    for k in range(half + 1):
        for f in range(features):
            if k < half and k < f <= k + half:
                other = k + half + 1
            elif 1 <= (k - f) % features <= half:
                other = k
            else:
                continue
            a, b = min(f, other), max(f, other)
            rows.append(a * features - a * (a + 1) // 2 + b - a - 1)
            places.append(k * features + f)
    return rows, places


def kernel(**inputs):
    import numpy as np
    import concourse.bacc as bacc
    from concourse.bass_utils import run_bass_kernel_spmd

    features = 27
    n_pairs = features * (features - 1) // 2
    rows, places = pair_rows(features)
    w1 = np.asarray(inputs["W_top1"])
    w1_pairs = np.zeros(((features // 2 + 1) * features, w1.shape[1]), w1.dtype)
    w1_pairs[places] = w1[rows]

    names = ["r_bottom_output", "ids"] + [f"tbl_{i}" for i in range(features - 1)]
    arrays = {n: np.ascontiguousarray(inputs[n]) for n in names}
    arrays["w1_pairs"] = w1_pairs
    arrays["w1_bottom"] = np.ascontiguousarray(w1[n_pairs:])
    for n in ("b_top1", "W_top2", "b_top2", "W_top3"):
        arrays[n] = np.ascontiguousarray(inputs[n])

    nc = bacc.Bacc("TRN2", target_bir_lowering=False, num_devices=1)
    ap = {n: nc.dram_tensor(f"in_{n}", a.shape, mybir.dt.from_np(a.dtype), kind="ExternalInput").ap()
          for n, a in arrays.items()}
    batch = arrays["ids"].shape[0]
    y = nc.dram_tensor("y", (1, batch), mybir.dt.float32, kind="ExternalOutput").ap()
    dlrm_tower_kernel(nc, ap["r_bottom_output"], ap["ids"], [ap[f"tbl_{i}"] for i in range(features - 1)],
                      ap["w1_pairs"], ap["w1_bottom"], ap["b_top1"], ap["W_top2"], ap["b_top2"], ap["W_top3"], y)
    got = run_bass_kernel_spmd(nc, [{f"in_{n}": a for n, a in arrays.items()}], core_ids=[0])
    return got.results[0]["y"].reshape(batch, 1)
```

```python
import concourse.bass as bass
from concourse import mybir
from contextlib import ExitStack


LOOKED_UP = 8
CHUNKS = 8


def split_tables(rows):
    fit = [i for i, n in enumerate(rows) if n == min(rows) and n % CHUNKS == 0 and n // CHUNKS <= 128]
    looked_up = fit[:LOOKED_UP]
    return [i for i in range(len(rows)) if i not in looked_up], looked_up


def dlrm_tower_kernel(nc, r_dram, ids_dram, tables, w1_pairs_dram, w1_bottom_dram, b1_dram, w2_dram, b2_dram,
                      w3_dram, y_dram):
    fp32, fp32r, fp16, i32 = mybir.dt.float32, mybir.dt.float32r, mybir.dt.float16, mybir.dt.int32
    ALU = mybir.AluOpType
    ACT = mybir.ActivationFunctionType

    BATCH, NTAB = ids_dram.shape
    D = r_dram.shape[1]
    NF = NTAB + 1
    GATHERED, LOOKUPS = split_tables([t.shape[0] for t in tables])
    NX = len(LOOKUPS)
    NGF = 1 + len(GATHERED)
    ROWS = tables[LOOKUPS[0]].shape[0]
    RP = ROWS // CHUNKS
    FP = 32
    TB = 128
    TILES = BATCH // TB
    SG = TB // FP
    NQ = TB // SG
    HALF = NF // 2
    KC = HALF + 1
    CH = 3
    KR = KC * NF // CH
    H1 = w1_bottom_dram.shape[1]
    H2 = w2_dram.shape[1]
    O1, O2 = H1 // 128, H2 // 128
    OB = O1 // 2
    GRP = 4
    GROUPS = [list(range(a, min(a + GRP, NGF))) for a in range(0, NGF, GRP)]
    NG = len(GROUPS)
    ALL = [(t, g) for t in range(TILES) for g in range(NG)]
    LAG = 1
    EARLY = NX - LAG
    UQ = 8
    UNITS = NQ // UQ
    BANK = 512

    ctx = ExitStack()
    with ctx:
        def sb(name, shape, dt=fp32):
            return ctx.enter_context(nc.sbuf_tensor(name, shape, dt))

        def sem(name):
            return ctx.enter_context(nc.semaphore(name))

        ids_all = sb("ids_all", [TB, TILES, NTAB], i32)
        ids_half = sb("ids_half", [TB, TILES, NX], fp16)
        raw = sb("raw", [TB, TILES, NGF, D])
        feat_t = sb("feat_t", [D, TILES, NQ, SG, FP])
        gram = sb("gram", [128, NQ, KC])
        pairs = sb("pairs", [TB, KC, FP])
        packed = sb("packed", [TB, KC, NF])
        pairs_t = sb("pairs_t", [KR, CH, TB])
        w1_pairs = sb("w1_pairs", [KR, CH, H1])
        w1_bottom = sb("w1_bottom", [D, H1])
        w2 = sb("w2", [128, O1, H2])
        w3 = sb("w3", [128, O2])
        b1 = sb("b1", [128, O1])
        b2 = sb("b2", [128, O2])
        h1 = sb("h1", [128, O1, TB])
        h2 = sb("h2", [128, O2, TB])
        y_row = sb("y_row", [1, BATCH])
        ident = sb("ident", [128, 128])
        ident_half = sb("ident_half", [128, 128], fp16)
        second = sb("second", [128, UQ, HALF], i32)
        row_int = sb("row_int", [RP, CHUNKS], i32)
        row_no = sb("row_no", [RP, CHUNKS])
        act_warm = sb("act_warm", [128, 1])
        NSTAGE = 3
        table = [sb(f"table{i}", [RP, CHUNKS * D]) for i in range(NSTAGE)]
        high = [sb(f"high{i}", [RP, CHUNKS * D], fp32r) for i in range(2)]
        low = [sb(f"low{i}", [RP, CHUNKS * D], fp32r) for i in range(2)]
        ids_row = [sb(f"ids_row{i}", [RP, BATCH]) for i in range(2)]
        onehot = [sb(f"onehot{i}", [RP, CHUNKS, BATCH], fp32r) for i in range(2)]

        turn = [ctx.enter_context(nc.psum_tensor(f"turn{i}", [128, BANK], fp32)) for i in range(2)]
        dots = [ctx.enter_context(nc.psum_tensor(f"dots{i}", [128, UQ, 128], fp32)) for i in range(2)]
        acc = [ctx.enter_context(nc.psum_tensor(f"acc{i}", [128, BANK], fp32)) for i in range(2)]

        def bank(i):
            return dots[i][:, 0:BANK // 128, :].rearrange("p a b -> p (a b)")

        ids_in = sem("ids_in")
        bottom_in = sem("bottom_in")
        table_in = [sem(f"table_in{i}") for i in range(NSTAGE)]
        tower_in = sem("tower_in")
        group_in = [sem(f"group_in{t}_{g}") for t, g in ALL]
        pool_set = sem("pool_set")
        ident_ready = sem("ident_ready")
        mask_quadrant = sem("mask_quadrant")
        lookup_consts = sem("lookup_consts")
        mask_ready = sem("mask_ready")
        padding_ready = sem("padding_ready")
        high_ready = sem("high_ready")
        low_ready = sem("low_ready")
        ids_spread = sem("ids_spread")
        ids_row_ready = sem("ids_row_ready")
        onehot_ready = sem("onehot_ready")
        looked_up = sem("looked_up")
        lookup_copied = sem("lookup_copied")
        turned = sem("turned")
        group_copied = sem("group_copied")
        unit_done = sem("unit_done")
        first_copied = sem("first_copied")
        folded = sem("folded")
        pairs_ready = sem("pairs_ready")
        packed_ready = sem("packed_ready")
        pairs_turned = sem("pairs_turned")
        pairs_t_ready = sem("pairs_t_ready")
        acc1_done = sem("acc1_done")
        h1_act = sem("h1_act")
        h1_dve = sem("h1_dve")
        acc2_done = sem("acc2_done")
        h2_ready = sem("h2_ready")
        y_done = sem("y_done")
        y_ready = sem("y_ready")
        y_out = sem("y_out")
        TOWER = 6 * 16

        block = ctx.enter_context(nc.Block())

        @block.sync
        def _(sp):
            def load_table(x):
                source = tables[LOOKUPS[x]].rearrange("(p c) d -> p (c d)", c=CHUNKS)
                sp.dma_start(table[x % NSTAGE][:], source).then_inc(table_in[x % NSTAGE], 16)

            sp.dma_start(ids_all[:], ids_dram.rearrange("(t p) f -> p t f", p=TB)).then_inc(ids_in, 16)
            for x in range(NSTAGE):
                load_table(x)
            sp.dma_start(raw[:, :, 0, :], r_dram.rearrange("(t p) d -> p t d", p=TB)).then_inc(bottom_in, 16)
            for x in range(NSTAGE, NX):
                sp.wait_ge(low_ready, x - NSTAGE + 1)
                load_table(x)
            sp.dma_start(w1_pairs[:], w1_pairs_dram.rearrange("(c k) n -> k c n", c=CH)).then_inc(tower_in, 16)
            sp.dma_start(w1_bottom[:], w1_bottom_dram).then_inc(tower_in, 16)
            sp.dma_start(w2[:], w2_dram.rearrange("(c p) n -> p c n", p=128)).then_inc(tower_in, 16)
            with nc.allow_non_contiguous_dma(reason="one column of a few hundred values, once"):
                sp.dma_start(w3[:], w3_dram.rearrange("(c p) one -> p (c one)", p=128)).then_inc(tower_in, 16)
                sp.dma_start(b1[:], b1_dram.rearrange("(c p) -> p c", p=128)).then_inc(tower_in, 16)
                sp.dma_start(b2[:], b2_dram.rearrange("(c p) -> p c", p=128)).then_inc(tower_in, 16)
            sp.wait_ge(y_ready, TILES)
            sp.dma_start(y_dram, y_row[:]).then_inc(y_out, 16)
            sp.wait_ge(y_out, 16)

        @block.gpsimd
        def _(pool):
            nc.gpsimd.memset(ident[:], 1.0)
            nc.gpsimd.memset(second[0:FP], 1).then_inc(pool_set, 1)
            pool.wait_ge(pool_set, 1)
            nc.gpsimd.affine_select(out=ident[:], in_=ident[:], compare_op=ALU.is_equal, fill=0.0, base=0,
                                    pattern=[[-1, 128]], channel_multiplier=1).then_inc(ident_ready, 1)
            nc.gpsimd.iota(row_int[:], pattern=[[1, CHUNKS]], base=0, channel_multiplier=CHUNKS).then_inc(ident_ready, 1)
            nc.gpsimd.affine_select(out=second[0:FP], in_=second[0:FP], compare_op=ALU.is_gt, fill=0.0, base=0,
                                    pattern=[[0, UQ], [-1, HALF]], channel_multiplier=1).then_inc(pool_set, 1)
            pool.wait_ge(pool_set, 2)
            nc.gpsimd.affine_select(out=second[0:FP], in_=second[0:FP], compare_op=ALU.is_ge, fill=0.0, base=HALF,
                                    pattern=[[0, UQ], [1, HALF]], channel_multiplier=-1).then_inc(mask_quadrant, 1)
            pool.wait_ge(ids_in, 16)
            for k, (t, g) in enumerate(ALL):
                for f in GROUPS[g]:
                    if f > 0:
                        i = GATHERED[f - 1]
                        nc.gpsimd.indirect_dma_start(
                            out=raw[:, t, f, :], out_offset=None, in_=tables[i],
                            in_offset=bass.IndirectOffsetOnAxis(ap=ids_all[:, t, i:i + 1], axis=0),
                        ).then_inc(group_in[k], 16)

        @block.scalar
        def _(act):
            nc.scalar.activation(act_warm[:], nc.const_aps.tensor(0.0, (128, 1)), ACT.Relu)

            def take_high(x):
                act.wait_ge(table_in[x % NSTAGE], 16 * (x // NSTAGE + 1))
                if x >= 2:
                    act.wait_ge(looked_up, x - 1)
                nc.scalar.copy(high[x % 2][:], table[x % NSTAGE][:]).then_inc(high_ready, 1)

            def copy_ids_row(x):
                act.wait_ge(ids_spread, x + 1)
                if x >= 2:
                    act.wait_ge(onehot_ready, CHUNKS * (x - 1))
                nc.scalar.copy(ids_row[x % 2][:], bank(x % 2)[0:RP, :]).then_inc(ids_row_ready, 1)

            def copy_lookup(x):
                act.wait_ge(looked_up, x + 1)
                nc.scalar.copy(feat_t[:, :, :, :, NGF + x].rearrange("d t q s -> d t s q"),
                               acc[x % 2][:].rearrange("d (t s q) -> d t s q", t=TILES, s=SG)).then_inc(lookup_copied, 1)

            def copy_group(k):
                t, g = ALL[k]
                fs = GROUPS[g]
                act.wait_ge(turned, k + 1)
                nc.scalar.copy(feat_t[:, t, :, :, fs[0]:fs[-1] + 1].rearrange("d q s f -> d f s q"),
                               turn[k % 2][:, 0:len(fs) * TB].rearrange("d (f s q) -> d f s q", s=SG, q=NQ),
                               ).then_inc(group_copied, 1)

            def copy_first(t, u):
                act.wait_ge(unit_done, t * UNITS + u + 1)
                for s in range(SG):
                    own = slice(s * FP, (s + 1) * FP)
                    last = nc.scalar.copy(gram[own, u * UQ:(u + 1) * UQ, :], dots[u % 2][own, :, s * NF:s * NF + KC])
                last.then_inc(first_copied, 1)

            def relu1(t):
                act.wait_ge(acc1_done, 2 * t + 1)
                for o in range(OB):
                    last = nc.scalar.activation(h1[:, o, :], acc[0][:, o * TB:(o + 1) * TB], ACT.Relu,
                                                bias=b1[:, o:o + 1])
                last.then_inc(h1_act, 1)

            def relu2(t):
                act.wait_ge(acc2_done, t + 1)
                for o in range(O2):
                    last = nc.scalar.activation(h2[:, o, :], acc[0][:, o * TB:(o + 1) * TB], ACT.Relu,
                                                bias=b2[:, o:o + 1])
                last.then_inc(h2_ready, 1)

            for x in range(2):
                take_high(x)
                copy_ids_row(x)
            for x in range(NX):
                copy_lookup(x)
                if x + 2 < NX:
                    take_high(x + 2)
                    copy_ids_row(x + 2)
                if x >= LAG:
                    copy_group(x - LAG)
            for k in range(EARLY, NG):
                copy_group(k)
            act.wait_ge(tower_in, TOWER)
            for t in range(TILES):
                copy_first(t, 0)
                if t > 0:
                    relu2(t - 1)
                for u in range(1, UNITS):
                    copy_first(t, u)
                for k in range(max(EARLY, (t + 1) * NG), min((t + 2) * NG, len(ALL))):
                    copy_group(k)
                relu1(t)
            relu2(TILES - 1)

        @block.vector
        def _(dve):
            dve.wait_ge(ids_in, 16)
            dve.wait_ge(ident_ready, 2)
            for x, i in enumerate(LOOKUPS):
                nc.vector.tensor_copy(ids_half[:, :, x:x + 1], ids_all[:, :, i:i + 1])
            nc.vector.tensor_copy(row_no[:], row_int[:])
            nc.vector.tensor_copy(ident_half[:], ident[:]).then_inc(lookup_consts, 1)

            for x in range(NX):
                dve.wait_ge(high_ready, x + 1)
                nc.vector.tensor_tensor(low[x % 2][:], table[x % NSTAGE][:], high[x % 2][:].bitcast(fp32),
                                        ALU.subtract).then_inc(low_ready, 1)
                dve.wait_ge(ids_row_ready, x + 1)
                if x == 0:
                    dve.wait_ge(lookup_consts, 1)
                if x >= 2:
                    dve.wait_ge(looked_up, x - 1)
                for c in range(CHUNKS):
                    nc.vector.tensor_scalar(onehot[x % 2][:, c, :], ids_row[x % 2][:], row_no[:, c:c + 1], None,
                                            ALU.is_equal).then_inc(onehot_ready, 1)
                if x == 0:
                    nc.vector.memset(feat_t[:, :, :, :, NF:FP], 0.0).then_inc(padding_ready, 1)
            dve.wait_ge(mask_quadrant, 1)
            for s in range(1, SG):
                nc.vector.tensor_copy(second[s * FP:(s + 1) * FP], second[0:FP]).then_inc(mask_ready, 1)
            dve.wait_ge(mask_ready, SG - 1)

            def fold(t, u):
                dve.wait_ge(first_copied, t * UNITS + u + 1)
                for s in range(SG):
                    own = slice(s * FP, (s + 1) * FP)
                    last = nc.vector.copy_predicated(gram[own, u * UQ:(u + 1) * UQ, 0:HALF], second[own],
                                                     dots[u % 2][own, :, s * NF + KC:(s + 1) * NF])
                last.then_inc(folded, 1)

            def copy_y(t):
                dve.wait_ge(y_done, t + 1)
                nc.vector.tensor_copy(y_row[:, t * TB:(t + 1) * TB], acc[1][0:1, 0:TB]).then_inc(y_ready, 1)

            dve.wait_ge(tower_in, TOWER)
            for t in range(TILES):
                fold(t, 0)
                fold(t, 1)
                if t > 0:
                    copy_y(t - 1)
                for u in range(2, UNITS):
                    fold(t, u)
                dve.wait_ge(folded, (t + 1) * UNITS)
                nc.vector.transpose(pairs[:], gram[:].rearrange("p q k -> p k q")).then_inc(pairs_ready, 1)
                dve.wait_ge(pairs_ready, t + 1)
                nc.vector.tensor_copy(packed[:], pairs[:, :, 0:NF]).then_inc(packed_ready, 1)
                dve.wait_ge(pairs_turned, t + 1)
                nc.vector.tensor_copy(pairs_t[:].rearrange("k c b -> k (c b)"),
                                      bank(0)[0:KR, 0:CH * TB]).then_inc(pairs_t_ready, 1)
                dve.wait_ge(acc1_done, 2 * t + 2)
                for o in range(OB, O1):
                    at = (o - OB) * TB
                    last = nc.vector.tensor_scalar(h1[:, o, :], acc[1][:, at:at + TB], b1[:, o:o + 1], 0.0,
                                                   ALU.add, ALU.max)
                last.then_inc(h1_dve, 1)
            copy_y(TILES - 1)

        @block.tensor
        def _(pe):
            def spread_ids(x):
                if x >= 2:
                    pe.wait_ge(ids_row_ready, x - 1)
                for t in range(TILES):
                    last = nc.tensor.matmul(bank(x % 2)[0:RP, t * TB:(t + 1) * TB],
                                            ids_half[:, t, x:x + 1].broadcast_to((TB, RP)), ident_half[:],
                                            start=True, stop=True)
                last.then_inc(ids_spread, 1)

            def look_up(x):
                if x >= 2:
                    pe.wait_ge(lookup_copied, x - 1)
                pe.wait_ge(low_ready, x + 1)
                for c in range(CHUNKS):
                    pe.wait_ge(onehot_ready, x * CHUNKS + c + 1)
                    for part in (high, low):
                        last = nc.tensor.matmul(acc[x % 2][:], part[x % 2][:, c * D:(c + 1) * D],
                                                onehot[x % 2][:, c, :], start=(c == 0 and part is high),
                                                stop=(c == CHUNKS - 1 and part is low))
                last.then_inc(looked_up, 1)

            def turn_group(k):
                t, g = ALL[k]
                pe.wait_ge(group_in[k], 16 * (len(GROUPS[g]) - (g == 0)))
                if k == 0:
                    pe.wait_ge(bottom_in, 16)
                if k >= 2:
                    pe.wait_ge(group_copied, k - 1)
                for i, f in enumerate(GROUPS[g]):
                    last = nc.tensor.transpose(turn[k % 2][:, i * TB:(i + 1) * TB], raw[:, t, f, :], ident[:])
                last.then_inc(turned, 1)

            def gram_unit(t, u):
                if t * UNITS + u >= 2:
                    pe.wait_ge(folded, t * UNITS + u - 1)
                for i in range(UQ):
                    q = u * UQ + i
                    last = nc.tensor.matmul(dots[u % 2][:, i, 0:SG * NF],
                                            feat_t[:, t, q].rearrange("d s f -> d (s f)"),
                                            feat_t[:, t, q, :, 0:NF], start=True, stop=True)
                last.then_inc(unit_done, 1)

            def layer1(t):
                if t > 0:
                    pe.wait_ge(h2_ready, t)
                    pe.wait_ge(y_ready, t)
                bottom_t = feat_t[:, t, :, :, 0].rearrange("d q s -> d s q")
                for o in range(O1):
                    dst = acc[o // OB][:, (o % OB) * TB:(o % OB + 1) * TB]
                    out_cols = slice(o * 128, (o + 1) * 128)
                    nc.tensor.matmul(dst, w1_bottom[:, out_cols], bottom_t, start=True, stop=False)
                    if o == 0:
                        pe.wait_ge(pairs_t_ready, t + 1)
                    for c in range(CH):
                        last = nc.tensor.matmul(dst, w1_pairs[:, c, out_cols], pairs_t[:, c, :],
                                                start=False, stop=(c == CH - 1))
                    if o % OB == OB - 1:
                        last.then_inc(acc1_done, 1)

            def layer2(t):
                pe.wait_ge(h1_act, t + 1)
                pe.wait_ge(h1_dve, t + 1)
                for o in range(O2):
                    for c in range(O1):
                        last = nc.tensor.matmul(acc[0][:, o * TB:(o + 1) * TB], w2[:, c, o * 128:(o + 1) * 128],
                                                h1[:, c, :], start=(c == 0), stop=(c == O1 - 1))
                last.then_inc(acc2_done, 1)

            def layer3(t):
                pe.wait_ge(h2_ready, t + 1)
                for c in range(O2):
                    last = nc.tensor.matmul(acc[1][0:1, 0:TB], w3[:, c:c + 1], h2[:, c, :],
                                            start=(c == 0), stop=(c == O2 - 1))
                last.then_inc(y_done, 1)

            pe.wait_ge(lookup_consts, 1)
            for x in range(2):
                spread_ids(x)
            for x in range(NX):
                look_up(x)
                if x + 2 < NX:
                    spread_ids(x + 2)
                if x >= LAG:
                    turn_group(x - LAG)
            for k in range(EARLY, NG):
                turn_group(k)
            pe.wait_ge(lookup_copied, NX)
            pe.wait_ge(padding_ready, 1)
            pe.wait_ge(ids_row_ready, NX)
            pe.wait_ge(tower_in, TOWER)
            for t in range(TILES):
                pe.wait_ge(group_copied, (t + 1) * NG)
                gram_unit(t, 0)
                if t > 0:
                    layer2(t - 1)
                gram_unit(t, 1)
                if t > 0:
                    layer3(t - 1)
                gram_unit(t, 2)
                gram_unit(t, 3)
                for k in range(max(EARLY, (t + 1) * NG), min((t + 2) * NG, len(ALL))):
                    turn_group(k)
                pe.wait_ge(packed_ready, t + 1)
                for c in range(CH):
                    last = nc.tensor.transpose(bank(0)[0:KR, c * TB:(c + 1) * TB],
                                               packed[:].rearrange("b k f -> b (k f)")[:, c * KR:(c + 1) * KR],
                                               ident[:])
                last.then_inc(pairs_turned, 1)
                layer1(t)
            layer2(TILES - 1)
            layer3(TILES - 1)


def pair_rows(order):
    features = len(order)
    half = features // 2
    rows, places = [], []
    for k in range(half + 1):
        for f in range(features):
            if k < half and k < f <= k + half:
                other = k + half + 1
            elif 1 <= (k - f) % features <= half:
                other = k
            else:
                continue
            a, b = sorted((order[f], order[other]))
            rows.append(a * features - a * (a + 1) // 2 + b - a - 1)
            places.append(k * features + f)
    return rows, places


def kernel(**inputs):
    import numpy as np
    import concourse.bacc as bacc
    from concourse.bass_utils import run_bass_kernel_spmd

    features = np.asarray(inputs["ids"]).shape[1] + 1
    gathered, looked_up = split_tables([np.asarray(inputs[f"tbl_{i}"]).shape[0] for i in range(features - 1)])
    order = [0] + [i + 1 for i in gathered + looked_up]
    n_pairs = features * (features - 1) // 2
    rows, places = pair_rows(order)
    w1 = np.asarray(inputs["W_top1"])
    w1_pairs = np.zeros(((features // 2 + 1) * features, w1.shape[1]), w1.dtype)
    w1_pairs[places] = w1[rows]

    names = ["r_bottom_output", "ids"] + [f"tbl_{i}" for i in range(features - 1)]
    arrays = {n: np.ascontiguousarray(inputs[n]) for n in names}
    arrays["w1_pairs"] = w1_pairs
    arrays["w1_bottom"] = np.ascontiguousarray(w1[n_pairs:])
    for n in ("b_top1", "W_top2", "b_top2", "W_top3"):
        arrays[n] = np.ascontiguousarray(inputs[n])

    nc = bacc.Bacc("TRN2", target_bir_lowering=False, num_devices=1)
    ap = {n: nc.dram_tensor(f"in_{n}", a.shape, mybir.dt.from_np(a.dtype), kind="ExternalInput").ap()
          for n, a in arrays.items()}
    batch = arrays["ids"].shape[0]
    y = nc.dram_tensor("y", (1, batch), mybir.dt.float32, kind="ExternalOutput").ap()
    dlrm_tower_kernel(nc, ap["r_bottom_output"], ap["ids"], [ap[f"tbl_{i}"] for i in range(features - 1)],
                      ap["w1_pairs"], ap["w1_bottom"], ap["b_top1"], ap["W_top2"], ap["b_top2"], ap["W_top3"], y)
    got = run_bass_kernel_spmd(nc, [{f"in_{n}": a for n, a in arrays.items()}], core_ids=[0])
    return got.results[0]["y"].reshape(batch, 1)
```

```python
import concourse.bass as bass
from concourse import mybir
from contextlib import ExitStack


LOOKED_UP = 8
CHUNKS = 8


def split_tables(rows):
    fit = [i for i, n in enumerate(rows) if n == min(rows) and n % CHUNKS == 0 and n // CHUNKS <= 128]
    looked_up = fit[:LOOKED_UP]
    return [i for i in range(len(rows)) if i not in looked_up], looked_up


def dlrm_tower_kernel(nc, r_t_dram, ids_dram, ids_t_dram, tables, w1_pairs_dram, w1_bottom_dram, b1_dram, w2_dram,
                      b2_dram, w3_dram, y_dram):
    fp32, fp32r, fp16, i32 = mybir.dt.float32, mybir.dt.float32r, mybir.dt.float16, mybir.dt.int32
    ALU = mybir.AluOpType
    ACT = mybir.ActivationFunctionType

    BATCH, NTAB = ids_dram.shape
    D = r_t_dram.shape[0]
    NF = NTAB + 1
    GATHERED, LOOKUPS = split_tables([t.shape[0] for t in tables])
    NX = len(LOOKUPS)
    NGF = 1 + len(GATHERED)
    ROWS = tables[LOOKUPS[0]].shape[0]
    RP = ROWS // CHUNKS
    FP = 32
    TB = 128
    TILES = BATCH // TB
    SG = TB // FP
    NQ = TB // SG
    HALF = NF // 2
    KC = HALF + 1
    CH = 3
    KR = KC * NF // CH
    FIRST = -(-KR // NF)
    H1 = w1_bottom_dram.shape[1]
    H2 = w2_dram.shape[1]
    O1, O2 = H1 // 128, H2 // 128
    OB = O1 // 2
    GRP = 4
    GROUPS = [list(range(a, min(a + GRP, NGF))) for a in range(1, NGF, GRP)]
    NG = len(GROUPS)
    ALL = [(t, g) for t in range(TILES) for g in range(NG)]
    EARLY = NX
    FIRST_GROUPS = 3
    FILL = 2
    COLUMNS_FIRST = 2
    WAKE = 10
    UQ = 8
    UNITS = NQ // UQ
    GP = TB - (FP - NF)
    BANK = 512

    ctx = ExitStack()
    with ctx:
        def sb(name, shape, dt=fp32):
            return ctx.enter_context(nc.sbuf_tensor(name, shape, dt))

        def sem(name):
            return ctx.enter_context(nc.semaphore(name))

        ids_all = sb("ids_all", [TB, TILES, NTAB], i32)
        raw = sb("raw", [TB, TILES, len(GATHERED), D])
        bottom_t = sb("bottom_t", [D, BATCH])
        feat_t = sb("feat_t", [D, TILES, NQ, SG, FP])
        gram = sb("gram", [128, NQ, KC])
        pairs = sb("pairs", [TB, KC, FP])
        packed = sb("packed", [TB, KC, NF])
        pairs_t = sb("pairs_t", [KR, CH, TB])
        w1_pairs = sb("w1_pairs", [KR, CH, H1])
        w1_bottom = sb("w1_bottom", [D, H1])
        w2 = sb("w2", [128, O1, H2])
        w3 = sb("w3", [128, O2])
        b1 = sb("b1", [128, O1])
        b2 = sb("b2", [128, O2])
        h1 = sb("h1", [128, O1, TB])
        h2 = sb("h2", [128, O2, TB])
        y_row = sb("y_row", [1, BATCH])
        ident = sb("ident", [128, 128])
        second = sb("second", [128, UQ, HALF], i32)
        row_int = sb("row_int", [RP, CHUNKS], i32)
        row_no = sb("row_no", [RP, CHUNKS])
        last_row_neg = sb("last_row_neg", [RP, 1])
        act_warm = sb("act_warm", [128, 1])
        zeros = sb("zeros", [128, BANK], fp16)
        distance = sb("distance", [RP, BATCH])
        NSTAGE = 3
        PART = CHUNKS // 2 * D
        table = [sb(f"table{i}", [RP, CHUNKS * D]) for i in range(NSTAGE)]
        high = [sb(f"high{i}", [RP, CHUNKS * D], fp32r) for i in range(2)]
        low = [sb(f"low{i}", [RP, CHUNKS * D], fp32r) for i in range(2)]
        ids_row = [sb(f"ids_row{i}", [RP, BATCH], i32) for i in range(NSTAGE)]
        onehot = [sb(f"onehot{i}", [RP, CHUNKS, BATCH], fp32r) for i in range(2)]

        turn = [ctx.enter_context(nc.psum_tensor(f"turn{i}", [128, BANK], fp32)) for i in range(2)]
        dots = [ctx.enter_context(nc.psum_tensor(f"dots{i}", [128, UQ, 128], fp32)) for i in range(2)]
        acc = [ctx.enter_context(nc.psum_tensor(f"acc{i}", [128, BANK], fp32)) for i in range(2)]

        def bank(i):
            return dots[i][:, 0:BANK // 128, :].rearrange("p a b -> p (a b)")

        ids_in = sem("ids_in")
        bottom_in = sem("bottom_in")
        first_part_in = sem("first_part_in")
        first_part_high = sem("first_part_high")
        table_in = [sem(f"table_in{i}") for i in range(NSTAGE)]
        tower_in = sem("tower_in")
        group_in = [sem(f"group_in{t}_{g}") for t, g in ALL]
        pool_set = sem("pool_set")
        ident_ready = sem("ident_ready")
        mask_quadrant = sem("mask_quadrant")
        bottom_ready = sem("bottom_ready")
        zeros_ready = sem("zeros_ready")
        row_no_ready = sem("row_no_ready")
        distance_ready = sem("distance_ready")
        act_columns_ready = sem("act_columns_ready")
        mask_ready = sem("mask_ready")
        padding_ready = sem("padding_ready")
        high_ready = sem("high_ready")
        low_ready = sem("low_ready")
        ids_row_in = [sem(f"ids_row_in{i}") for i in range(NSTAGE)]
        onehot_ready = sem("onehot_ready")
        looked_up = sem("looked_up")
        lookup_copied = sem("lookup_copied")
        turned = sem("turned")
        group_copied = sem("group_copied")
        unit_done = sem("unit_done")
        first_copied = sem("first_copied")
        folded = sem("folded")
        pairs_ready = sem("pairs_ready")
        packed_ready = sem("packed_ready")
        pairs_turned = sem("pairs_turned")
        pairs_t_act = sem("pairs_t_act")
        pairs_t_dve = sem("pairs_t_dve")
        acc1_done = sem("acc1_done")
        h1_act = sem("h1_act")
        h1_dve = sem("h1_dve")
        acc2_done = sem("acc2_done")
        h2_ready = sem("h2_ready")
        y_done = sem("y_done")
        y_ready = sem("y_ready")
        y_out = sem("y_out")
        TOWER = 6 * 16

        def acc2(t, o):
            if t < TILES - 2:
                return dots[o][:, BANK // 128:, :].rearrange("p a b -> p (a b)")[:, 0:TB]
            if t == TILES - 2:
                return turn[0][:, o * TB:(o + 1) * TB]
            return turn[o][:, 0:TB]

        def acc3(t):
            return (turn[1][:, 0:TB] if t == TILES - 2 else acc2(t, 0))[0:1, :]

        def groups_after(x):
            return range(x - 1, EARLY) if x == NX - 1 else range(max(x - 1, 0), x)

        def groups_beside(t):
            return [k for k in range(EARLY, len(ALL)) if (0 if k < EARLY + FIRST_GROUPS else (k // NG) - 1) == t]

        block = ctx.enter_context(nc.Block())

        @block.sync
        def _(sp):
            def load_table(x):
                source = tables[LOOKUPS[x]].rearrange("(p c) d -> p (c d)", c=CHUNKS)
                if x == 0:
                    sp.dma_start(table[0][:, 0:PART], source[:, 0:PART]).then_inc(first_part_in, 16)
                    sp.dma_start(table[0][:, PART:], source[:, PART:]).then_inc(table_in[0], 16)
                else:
                    sp.dma_start(table[x % NSTAGE][:], source).then_inc(table_in[x % NSTAGE], 16)

            def load_ids(x):
                i = LOOKUPS[x]
                sp.dma_start(ids_row[x % NSTAGE][:], ids_t_dram[i:i + 1, :].broadcast_to((RP, BATCH)),
                             ).then_inc(ids_row_in[x % NSTAGE], 16)

            sp.dma_start(ids_all[:], ids_dram.rearrange("(t p) f -> p t f", p=TB)).then_inc(ids_in, 16)
            for x in range(NSTAGE):
                load_ids(x)
                load_table(x)
            sp.dma_start(bottom_t[:], r_t_dram).then_inc(bottom_in, 16)
            for x in range(NSTAGE, NX):
                sp.wait_ge(low_ready, x - NSTAGE + 1)
                load_table(x)
                sp.wait_ge(onehot_ready, (CHUNKS - 1) * (x - NSTAGE + 1))
                sp.wait_ge(distance_ready, x - NSTAGE + 1)
                load_ids(x)
            sp.dma_start(w1_pairs[:], w1_pairs_dram.rearrange("(c k) n -> k c n", c=CH)).then_inc(tower_in, 16)
            sp.dma_start(w1_bottom[:], w1_bottom_dram).then_inc(tower_in, 16)
            sp.dma_start(w2[:], w2_dram.rearrange("(c p) n -> p c n", p=128)).then_inc(tower_in, 16)
            with nc.allow_non_contiguous_dma(reason="one column of a few hundred values, once"):
                sp.dma_start(w3[:], w3_dram.rearrange("(c p) one -> p (c one)", p=128)).then_inc(tower_in, 16)
                sp.dma_start(b1[:], b1_dram.rearrange("(c p) -> p c", p=128)).then_inc(tower_in, 16)
                sp.dma_start(b2[:], b2_dram.rearrange("(c p) -> p c", p=128)).then_inc(tower_in, 16)
            sp.wait_ge(y_ready, TILES)
            sp.dma_start(y_dram, y_row[:]).then_inc(y_out, 16)
            sp.wait_ge(y_out, 16)

        @block.gpsimd
        def _(pool):
            nc.gpsimd.memset(ident[:], 1.0)
            nc.gpsimd.memset(second[0:FP], 1).then_inc(pool_set, 1)
            pool.wait_ge(pool_set, 1)
            nc.gpsimd.affine_select(out=ident[:], in_=ident[:], compare_op=ALU.is_equal, fill=0.0, base=0,
                                    pattern=[[-1, 128]], channel_multiplier=1).then_inc(ident_ready, 1)
            nc.gpsimd.iota(row_int[:], pattern=[[1, CHUNKS]], base=0,
                           channel_multiplier=CHUNKS).then_inc(ident_ready, 1)
            nc.gpsimd.affine_select(out=second[0:FP], in_=second[0:FP], compare_op=ALU.is_gt, fill=0.0, base=0,
                                    pattern=[[0, UQ], [-1, HALF]], channel_multiplier=1).then_inc(pool_set, 1)
            pool.wait_ge(pool_set, 2)
            nc.gpsimd.affine_select(out=second[0:FP], in_=second[0:FP], compare_op=ALU.is_ge, fill=0.0, base=HALF,
                                    pattern=[[0, UQ], [1, HALF]], channel_multiplier=-1).then_inc(mask_quadrant, 1)
            pool.wait_ge(ids_in, 16)
            for k, (t, g) in enumerate(ALL):
                for f in GROUPS[g]:
                    i = GATHERED[f - 1]
                    nc.gpsimd.indirect_dma_start(
                        out=raw[:, t, f - 1, :], out_offset=None, in_=tables[i],
                        in_offset=bass.IndirectOffsetOnAxis(ap=ids_all[:, t, i:i + 1], axis=0),
                    ).then_inc(group_in[k], 16)

        @block.scalar
        def _(act):
            nc.scalar.activation(act_warm[:], nc.const_aps.tensor(0.0, (128, 1)), ACT.Relu)

            def take_high(x):
                if x == 0:
                    act.wait_ge(first_part_in, 16)
                    nc.scalar.copy(high[0][:, 0:PART], table[0][:, 0:PART]).then_inc(first_part_high, 1)
                    act.wait_ge(table_in[0], 16)
                    nc.scalar.copy(high[0][:, PART:], table[0][:, PART:]).then_inc(high_ready, 1)
                    return
                act.wait_ge(table_in[x % NSTAGE], 16 * (x // NSTAGE + 1))
                if x >= 2:
                    act.wait_ge(looked_up, x - 1)
                nc.scalar.copy(high[x % 2][:], table[x % NSTAGE][:]).then_inc(high_ready, 1)

            def last_columns(x):
                if x == 0:
                    act.wait_ge(row_no_ready, 2)
                if x >= 2:
                    act.wait_ge(looked_up, x - 1)
                if x >= 1:
                    act.wait_ge(act_columns_ready, x)
                act.wait_ge(ids_row_in[x % NSTAGE], 16 * (x // NSTAGE + 1))
                nc.scalar.activation(distance[:], ids_row[x % NSTAGE][:], ACT.Abs,
                                     bias=last_row_neg[:]).then_inc(distance_ready, 1)
                act.wait_ge(distance_ready, x + 1)
                nc.scalar.activation(onehot[x % 2][:, CHUNKS - 1, :], distance[:], ACT.Relu, bias=1.0,
                                     scale=-1.0).then_inc(act_columns_ready, 1)

            def copy_lookup(x):
                act.wait_ge(looked_up, x + 1)
                nc.scalar.copy(feat_t[:, :, :, :, NGF + x].rearrange("d t q s -> d t s q"),
                               acc[x % 2][:].rearrange("d (t s q) -> d t s q", t=TILES, s=SG)).then_inc(lookup_copied, 1)

            def copy_group(k):
                t, g = ALL[k]
                fs = GROUPS[g]
                act.wait_ge(turned, k + 1)
                nc.scalar.copy(feat_t[:, t, :, :, fs[0]:fs[-1] + 1].rearrange("d q s f -> d f s q"),
                               turn[k % 2][:, 0:len(fs) * TB].rearrange("d (f s q) -> d f s q", s=SG, q=NQ),
                               ).then_inc(group_copied, 1)

            def copy_first(t, u):
                act.wait_ge(unit_done, t * UNITS + u + 1)
                for s in range(SG):
                    own = slice(s * FP, s * FP + NF)
                    nc.scalar.copy(gram[own, u * UQ:(u + 1) * UQ, :],
                                   dots[u % 2][own, :, s * NF:s * NF + KC]).then_inc(first_copied, 1)

            def relu1(t):
                act.wait_ge(acc1_done, 2 * t + 1)
                for o in range(OB):
                    last = nc.scalar.activation(h1[:, o, :], acc[0][:, o * TB:(o + 1) * TB], ACT.Relu,
                                                bias=b1[:, o:o + 1])
                last.then_inc(h1_act, 1)

            def relu2(t):
                for o in range(O2):
                    act.wait_ge(acc2_done, t * O2 + o + 1)
                    nc.scalar.activation(h2[:, o, :], acc2(t, o), ACT.Relu, bias=b2[:, o:o + 1]).then_inc(h2_ready, 1)

            take_high(0)
            last_columns(0)
            take_high(1)
            for x in range(NX):
                if x + 1 < NX:
                    last_columns(x + 1)
                copy_lookup(x)
                if x + 2 < NX:
                    take_high(x + 2)
                for k in groups_after(x):
                    copy_group(k)
            act.wait_ge(tower_in, TOWER)
            for t in range(TILES):
                for u in range(UNITS):
                    copy_first(t, u)
                if t > 0:
                    relu2(t - 1)
                if t == 0:
                    for k in groups_beside(t)[:FILL]:
                        copy_group(k)
                act.wait_ge(pairs_turned, 2 * t + 1)
                nc.scalar.copy(pairs_t[:, 0, :], bank(0)[0:KR, 0:TB]).then_inc(pairs_t_act, 1)
                between = groups_beside(t)[FILL if t == 0 else 0:]
                for k in between[:3]:
                    copy_group(k)
                relu1(t)
                for k in between[3:]:
                    copy_group(k)
            relu2(TILES - 1)

        @block.vector
        def _(dve):
            def clear_padding(t):
                nc.vector.memset(feat_t[:, t, :, :, NF:FP], 0.0).then_inc(padding_ready, 1)

            nc.vector.memset(zeros[:], 0.0).then_inc(zeros_ready, 1)
            nc.vector.memset(gram[:], 0.0).then_inc(padding_ready, 1)
            clear_padding(0)
            clear_padding(1)
            dve.wait_ge(ident_ready, 2)
            nc.vector.tensor_copy(row_no[:], row_int[:]).then_inc(row_no_ready, 1)
            nc.vector.tensor_scalar(last_row_neg[:], row_int[:, CHUNKS - 1:CHUNKS], -1.0, None,
                                    ALU.mult).then_inc(row_no_ready, 1)

            def take_low(x):
                if x == 0:
                    dve.wait_ge(first_part_high, 1)
                dve.wait_ge(high_ready, x + 1)
                nc.vector.tensor_tensor(low[x % 2][:], table[x % NSTAGE][:], high[x % 2][:].bitcast(fp32),
                                        ALU.subtract).then_inc(low_ready, 1)

            def columns(x):
                dve.wait_ge(ids_row_in[x % NSTAGE], 16 * (x // NSTAGE + 1))
                if x == 0:
                    dve.wait_ge(row_no_ready, 1)
                if x >= 2:
                    dve.wait_ge(looked_up, x - 1)
                for c in range(CHUNKS - 1):
                    nc.vector.tensor_scalar(onehot[x % 2][:, c, :], ids_row[x % NSTAGE][:], row_no[:, c:c + 1], None,
                                            ALU.is_equal).then_inc(onehot_ready, 1)

            for x in range(NX):
                if x < COLUMNS_FIRST:
                    columns(x)
                    take_low(x)
                else:
                    take_low(x)
                    columns(x)
            dve.wait_ge(bottom_in, 16)
            nc.vector.tensor_copy(feat_t[:, :, :, :, 0].rearrange("d t q s -> d t s q"),
                                  bottom_t[:].rearrange("d (t s q) -> d t s q", t=TILES, s=SG)).then_inc(bottom_ready, 1)
            dve.wait_ge(mask_quadrant, 1)
            for s in range(1, SG):
                nc.vector.tensor_copy(second[s * FP:(s + 1) * FP], second[0:FP]).then_inc(mask_ready, 1)
            dve.wait_ge(mask_ready, SG - 1)

            def fold(t, u):
                for s in range(SG):
                    own = slice(s * FP, s * FP + NF)
                    dve.wait_ge(first_copied, (t * UNITS + u) * SG + s + 1)
                    last = nc.vector.copy_predicated(gram[own, u * UQ:(u + 1) * UQ, 0:HALF], second[own],
                                                     dots[u % 2][own, :, s * NF + KC:(s + 1) * NF])
                last.then_inc(folded, 1)

            def copy_y(t):
                dve.wait_ge(y_done, t + 1)
                nc.vector.tensor_copy(y_row[:, t * TB:(t + 1) * TB], acc3(t)).then_inc(y_ready, 1)

            dve.wait_ge(tower_in, TOWER)
            for t in range(TILES):
                for u in range(UNITS):
                    fold(t, u)
                dve.wait_ge(folded, (t + 1) * UNITS)
                for i, (a, b) in enumerate([(0, FIRST), (FIRST, KC)]):
                    nc.vector.transpose(pairs[:, a:b],
                                        gram[:, :, a:b].rearrange("p q k -> p k q")).then_inc(pairs_ready, 1)
                    dve.wait_ge(pairs_ready, 2 * t + i + 1)
                    nc.vector.tensor_copy(packed[:, a:b], pairs[:, a:b, 0:NF]).then_inc(packed_ready, 1)
                dve.wait_ge(pairs_turned, 2 * t + 2)
                nc.vector.tensor_copy(pairs_t[:, 1:, :].rearrange("k c b -> k (c b)"),
                                      bank(1)[0:KR, 0:(CH - 1) * TB]).then_inc(pairs_t_dve, 1)
                if t > 0:
                    copy_y(t - 1)
                dve.wait_ge(acc1_done, 2 * t + 2)
                for o in range(OB, O1):
                    at = (o - OB) * TB
                    last = nc.vector.tensor_scalar(h1[:, o, :], acc[1][:, at:at + TB], b1[:, o:o + 1], 0.0,
                                                   ALU.add, ALU.max)
                last.then_inc(h1_dve, 1)
                if t + 2 < TILES:
                    clear_padding(t + 2)
            copy_y(TILES - 1)

        @block.tensor
        def _(pe):
            def look_up(x):
                if x >= 2:
                    pe.wait_ge(lookup_copied, x - 1)

                def product(c, part, ready):
                    if c == CHUNKS - 1:
                        pe.wait_ge(act_columns_ready, x + 1)
                    else:
                        pe.wait_ge(onehot_ready, x * (CHUNKS - 1) + c + 1)
                    if x == 0 and c * D < PART and part is high:
                        pe.wait_ge(first_part_high, 1)
                    else:
                        pe.wait_ge(ready, x + 1)
                    return nc.tensor.matmul(acc[x % 2][:], part[x % 2][:, c * D:(c + 1) * D], onehot[x % 2][:, c, :],
                                            start=(c == 0 and part is high), stop=(c == CHUNKS - 1 and part is low))

                if x < COLUMNS_FIRST:
                    for c in range(CHUNKS):
                        product(c, high, high_ready)
                    for c in range(CHUNKS):
                        last = product(c, low, low_ready)
                else:
                    for c in range(CHUNKS):
                        product(c, high, high_ready)
                        last = product(c, low, low_ready)
                last.then_inc(looked_up, 1)

            def turn_group(k):
                t, g = ALL[k]
                pe.wait_ge(group_in[k], 16 * len(GROUPS[g]))
                if k == 0:
                    pe.wait_ge(ident_ready, 1)
                if k >= 2:
                    pe.wait_ge(group_copied, k - 1)
                for i, f in enumerate(GROUPS[g]):
                    last = nc.tensor.transpose(turn[k % 2][:, i * TB:(i + 1) * TB], raw[:, t, f - 1, :], ident[:])
                last.then_inc(turned, 1)

            def gram_unit(t, u):
                if t * UNITS + u >= 2:
                    pe.wait_ge(folded, t * UNITS + u - 1)
                for i in range(UQ):
                    q = u * UQ + i
                    last = nc.tensor.matmul(dots[u % 2][0:GP, i, 0:SG * NF],
                                            feat_t[:, t, q].rearrange("d s f -> d (s f)")[:, 0:GP],
                                            feat_t[:, t, q, :, 0:NF], start=True, stop=True)
                last.then_inc(unit_done, 1)

            def turn_pairs(t, c):
                pe.wait_ge(packed_ready, 2 * t + 1 if c == 0 else 2 * t + 2)
                dst = bank(0)[0:KR, 0:TB] if c == 0 else bank(1)[0:KR, (c - 1) * TB:c * TB]
                last = nc.tensor.transpose(dst, packed[:].rearrange("b k f -> b (k f)")[:, c * KR:(c + 1) * KR],
                                           ident[:])
                if c != 1:
                    last.then_inc(pairs_turned, 1)

            def acc1(o):
                return acc[o // OB][:, (o % OB) * TB:(o % OB + 1) * TB]

            def layer1_bottom(t):
                if t > 0:
                    pe.wait_ge(h1_act, t)
                    pe.wait_ge(h1_dve, t)
                for o in range(O1):
                    nc.tensor.matmul(acc1(o), w1_bottom[:, o * 128:(o + 1) * 128],
                                     bottom_t[:, t * TB:(t + 1) * TB],
                                     start=(o % OB == 0), stop=False, skip_group_check=True)

            def layer1_pairs(t, o, chunks):
                pe.wait_ge(pairs_t_act, t + 1)
                if chunks[-1] > 0:
                    pe.wait_ge(pairs_t_dve, t + 1)
                for c in chunks:
                    last = nc.tensor.matmul(acc1(o), w1_pairs[:, c, o * 128:(o + 1) * 128], pairs_t[:, c, :],
                                            start=False, stop=(c == CH - 1), skip_group_check=True)
                if chunks[-1] == CH - 1 and o % OB == OB - 1:
                    last.then_inc(acc1_done, 1)

            def layer2(t, halves=(0, 1), outs=range(O2)):
                if 0 in halves and 0 in outs:
                    if t > 0:
                        pe.wait_ge(y_ready, t)
                    if t < TILES - 2:
                        pe.wait_ge(folded, (t + 2) * UNITS - 1)
                    elif t == TILES - 2:
                        pe.wait_ge(group_copied, len(ALL) - 1)
                    else:
                        pe.wait_ge(group_copied, len(ALL))
                shared = t == TILES - 2
                for half in halves:
                    if half == 0:
                        pe.wait_ge(h1_act, t + 1)
                    else:
                        pe.wait_ge(h1_dve, t + 1)
                    for o in outs:
                        if half == 0 and o == 1 and t < TILES - 2:
                            pe.wait_ge(folded, (t + 2) * UNITS)
                        for c in range(half * OB, (half + 1) * OB):
                            last = nc.tensor.matmul(acc2(t, o), w2[:, c, o * 128:(o + 1) * 128], h1[:, c, :],
                                                    start=(c == 0 and not (shared and o > 0)), stop=(c == O1 - 1),
                                                    skip_group_check=shared)
                        if half == 1 and not shared:
                            last.then_inc(acc2_done, 1)
                if shared and 1 in halves:
                    last.then_inc(acc2_done, O2)

            def layer3(t):
                for c in range(O2):
                    pe.wait_ge(h2_ready, t * O2 + c + 1)
                    last = nc.tensor.matmul(acc3(t), w3[:, c:c + 1], h2[:, c, :], start=(c == 0), stop=(c == O2 - 1))
                last.then_inc(y_done, 1)

            def wake(n):
                for _ in range(n):
                    nc.tensor.matmul(turn[0][:], zeros[:, 0:128], zeros[:], start=True, stop=True)

            pe.wait_ge(zeros_ready, 1)
            wake(WAKE)
            for x in range(NX):
                look_up(x)
                for k in groups_after(x):
                    turn_group(k)
            pe.wait_ge(lookup_copied, NX)
            pe.wait_ge(bottom_ready, 1)
            pe.wait_ge(tower_in, TOWER)
            for t in range(TILES):
                pe.wait_ge(group_copied, (t + 1) * NG)
                pe.wait_ge(padding_ready, t + 2)
                if t > 1:
                    pe.wait_ge(y_ready, t - 1)
                for u in range(UNITS):
                    gram_unit(t, u)
                layer1_bottom(t)
                if t == TILES - 1:
                    layer2(t - 1, [1])
                elif t > 0:
                    layer2(t - 1)
                if t == 0:
                    for k in groups_beside(t)[:FILL]:
                        turn_group(k)
                pe.wait_ge(folded, (t + 1) * UNITS)
                between = groups_beside(t)[FILL if t == 0 else 0:]
                turn_pairs(t, 0)
                if t > 0:
                    layer3(t - 1)
                else:
                    turn_group(between[0])
                layer1_pairs(t, 0, [0])
                for c in range(1, CH):
                    turn_pairs(t, c)
                for k in between[0 if t > 0 else 1:2]:
                    turn_group(k)
                for o in range(1, O1):
                    layer1_pairs(t, o, [0])
                for o in range(O1):
                    layer1_pairs(t, o, range(1, CH))
                    for k in between[2 + o:3 + o]:
                        if k < len(ALL) - 1:
                            turn_group(k)
                if t == TILES - 2:
                    layer2(t, [0], [0])
                    turn_group(len(ALL) - 1)
                    layer2(t, [0], range(1, O2))
            layer2(TILES - 1)
            layer3(TILES - 1)


def pair_rows(order):
    features = len(order)
    half = features // 2
    rows, places = [], []
    for k in range(half + 1):
        for f in range(features):
            if k < half and k < f <= k + half:
                other = k + half + 1
            elif 1 <= (k - f) % features <= half:
                other = k
            else:
                continue
            a, b = sorted((order[f], order[other]))
            rows.append(a * features - a * (a + 1) // 2 + b - a - 1)
            places.append(k * features + f)
    return rows, places


def kernel(**inputs):
    import numpy as np
    import concourse.bacc as bacc
    from concourse.bass_utils import run_bass_kernel_spmd

    features = np.asarray(inputs["ids"]).shape[1] + 1
    gathered, looked_up = split_tables([np.asarray(inputs[f"tbl_{i}"]).shape[0] for i in range(features - 1)])
    order = [0] + [i + 1 for i in gathered + looked_up]
    n_pairs = features * (features - 1) // 2
    rows, places = pair_rows(order)
    w1 = np.asarray(inputs["W_top1"])
    w1_pairs = np.zeros(((features // 2 + 1) * features, w1.shape[1]), w1.dtype)
    w1_pairs[places] = w1[rows]

    names = ["ids"] + [f"tbl_{i}" for i in range(features - 1)]
    arrays = {n: np.ascontiguousarray(inputs[n]) for n in names}
    arrays["r_t"] = np.ascontiguousarray(np.asarray(inputs["r_bottom_output"]).T)
    arrays["ids_t"] = np.ascontiguousarray(np.asarray(inputs["ids"]).T)
    arrays["w1_pairs"] = w1_pairs
    arrays["w1_bottom"] = np.ascontiguousarray(w1[n_pairs:])
    for n in ("b_top1", "W_top2", "b_top2", "W_top3"):
        arrays[n] = np.ascontiguousarray(inputs[n])

    nc = bacc.Bacc("TRN2", target_bir_lowering=False, num_devices=1)
    ap = {n: nc.dram_tensor(f"in_{n}", a.shape, mybir.dt.from_np(a.dtype), kind="ExternalInput").ap()
          for n, a in arrays.items()}
    batch = arrays["ids"].shape[0]
    y = nc.dram_tensor("y", (1, batch), mybir.dt.float32, kind="ExternalOutput").ap()
    dlrm_tower_kernel(nc, ap["r_t"], ap["ids"], ap["ids_t"], [ap[f"tbl_{i}"] for i in range(features - 1)],
                      ap["w1_pairs"], ap["w1_bottom"], ap["b_top1"], ap["W_top2"], ap["b_top2"], ap["W_top3"], y)
    got = run_bass_kernel_spmd(nc, [{f"in_{n}": a for n, a in arrays.items()}], core_ids=[0])
    return got.results[0]["y"].reshape(batch, 1)
```
